# Optimizing a Trainium2 kernel written in Bass

```python
import numpy as np
import jax
import jax.numpy as jnp

def _softmax(x, axis=-1):
    return jax.nn.softmax(x, axis=axis)

def _gelu(x):
    return jax.nn.gelu(x, approximate=True)

def _silu(x):
    return jax.nn.silu(x)

def _sigmoid(x):
    return jax.nn.sigmoid(x)

def _layernorm(x, axis=-1, eps=1e-05):
    m = jnp.mean(x, axis=axis, keepdims=True)
    v = jnp.var(x, axis=axis, keepdims=True)
    return (x - m) / jnp.sqrt(v + eps)

def _scatter_add(tgt, idx, src, axis=0):
    return tgt.at[idx].add(src)

def _segment_sum(src, seg, n):
    return jax.ops.segment_sum(src, seg, n)
kernel_name = 'mk_dlrm_tower_d1_rec_r8_8e6c21'

def setup_inputs(seed: int=0):
    np.random.seed(seed)
    _w = jnp.asarray

    def _rec_inputs():
        import jax
        import jax.numpy as jnp
        _tk = jax.random.key(seed)
        ids = jnp.stack([jax.random.randint(jax.random.fold_in(_tk, 200 + f), (2048,), 0, v, jnp.int32) for f, v in enumerate([12500, 1250, 12500, 125000, 12500, 12500, 1000, 1250, 1250, 1000, 1250, 12500, 1250, 12500, 12500, 1000, 1000, 1000, 1000, 12500, 1000, 1250, 1000, 1250, 1250, 1000])], axis=1)
        tbl_0 = 0.05 * jax.random.normal(jax.random.fold_in(_tk, 500 + 0), (12500, 128), jnp.float32)
        tbl_1 = 0.05 * jax.random.normal(jax.random.fold_in(_tk, 500 + 1), (1250, 128), jnp.float32)
        tbl_2 = 0.05 * jax.random.normal(jax.random.fold_in(_tk, 500 + 2), (12500, 128), jnp.float32)
        tbl_3 = 0.05 * jax.random.normal(jax.random.fold_in(_tk, 500 + 3), (125000, 128), jnp.float32)
        tbl_4 = 0.05 * jax.random.normal(jax.random.fold_in(_tk, 500 + 4), (12500, 128), jnp.float32)
        tbl_5 = 0.05 * jax.random.normal(jax.random.fold_in(_tk, 500 + 5), (12500, 128), jnp.float32)
        tbl_6 = 0.05 * jax.random.normal(jax.random.fold_in(_tk, 500 + 6), (1000, 128), jnp.float32)
        tbl_7 = 0.05 * jax.random.normal(jax.random.fold_in(_tk, 500 + 7), (1250, 128), jnp.float32)
        tbl_8 = 0.05 * jax.random.normal(jax.random.fold_in(_tk, 500 + 8), (1250, 128), jnp.float32)
        tbl_9 = 0.05 * jax.random.normal(jax.random.fold_in(_tk, 500 + 9), (1000, 128), jnp.float32)
        tbl_10 = 0.05 * jax.random.normal(jax.random.fold_in(_tk, 500 + 10), (1250, 128), jnp.float32)
        tbl_11 = 0.05 * jax.random.normal(jax.random.fold_in(_tk, 500 + 11), (12500, 128), jnp.float32)
        tbl_12 = 0.05 * jax.random.normal(jax.random.fold_in(_tk, 500 + 12), (1250, 128), jnp.float32)
        tbl_13 = 0.05 * jax.random.normal(jax.random.fold_in(_tk, 500 + 13), (12500, 128), jnp.float32)
        tbl_14 = 0.05 * jax.random.normal(jax.random.fold_in(_tk, 500 + 14), (12500, 128), jnp.float32)
        tbl_15 = 0.05 * jax.random.normal(jax.random.fold_in(_tk, 500 + 15), (1000, 128), jnp.float32)
        tbl_16 = 0.05 * jax.random.normal(jax.random.fold_in(_tk, 500 + 16), (1000, 128), jnp.float32)
        tbl_17 = 0.05 * jax.random.normal(jax.random.fold_in(_tk, 500 + 17), (1000, 128), jnp.float32)
        tbl_18 = 0.05 * jax.random.normal(jax.random.fold_in(_tk, 500 + 18), (1000, 128), jnp.float32)
        tbl_19 = 0.05 * jax.random.normal(jax.random.fold_in(_tk, 500 + 19), (12500, 128), jnp.float32)
        tbl_20 = 0.05 * jax.random.normal(jax.random.fold_in(_tk, 500 + 20), (1000, 128), jnp.float32)
        tbl_21 = 0.05 * jax.random.normal(jax.random.fold_in(_tk, 500 + 21), (1250, 128), jnp.float32)
        tbl_22 = 0.05 * jax.random.normal(jax.random.fold_in(_tk, 500 + 22), (1000, 128), jnp.float32)
        tbl_23 = 0.05 * jax.random.normal(jax.random.fold_in(_tk, 500 + 23), (1250, 128), jnp.float32)
        tbl_24 = 0.05 * jax.random.normal(jax.random.fold_in(_tk, 500 + 24), (1250, 128), jnp.float32)
        tbl_25 = 0.05 * jax.random.normal(jax.random.fold_in(_tk, 500 + 25), (1000, 128), jnp.float32)
        _rk = jax.random.fold_in(_tk, 7)
        r_dense_features = -0.000520686 + 1.00062 * jax.random.normal(jax.random.fold_in(_rk, 101), (2048, 128), jnp.float32)
        W_top1 = 0.0405887 * jax.random.normal(jax.random.fold_in(_tk, 801), (607, 512), jnp.float32)
        W_top2 = 0.0441942 * jax.random.normal(jax.random.fold_in(_tk, 802), (512, 256), jnp.float32)
        W_top3 = 0.0625 * jax.random.normal(jax.random.fold_in(_tk, 803), (256, 1), jnp.float32)
        b_top1 = jnp.zeros((512,), jnp.float32)
        b_top2 = jnp.zeros((256,), jnp.float32)
        return (r_dense_features, ids, tbl_0, tbl_1, tbl_2, tbl_3, tbl_4, tbl_5, tbl_6, tbl_7, tbl_8, tbl_9, tbl_10, tbl_11, tbl_12, tbl_13, tbl_14, tbl_15, tbl_16, tbl_17, tbl_18, tbl_19, tbl_20, tbl_21, tbl_22, tbl_23, tbl_24, tbl_25, W_top1, b_top1, W_top2, b_top2, W_top3)
    r_dense_features, ids, tbl_0, tbl_1, tbl_2, tbl_3, tbl_4, tbl_5, tbl_6, tbl_7, tbl_8, tbl_9, tbl_10, tbl_11, tbl_12, tbl_13, tbl_14, tbl_15, tbl_16, tbl_17, tbl_18, tbl_19, tbl_20, tbl_21, tbl_22, tbl_23, tbl_24, tbl_25, W_top1, b_top1, W_top2, b_top2, W_top3 = _rec_inputs()

    def _L0_rec_setup():
        import jax, jax.numpy as jnp
        import numpy as np
        B, F, D = (2048, 26, 128)
        key = jax.random.key(seed)
        k1, k2 = jax.random.split(key)
        dense_features = jax.random.normal(k1, (B, D), dtype=jnp.float32)
        sparse_values = jax.random.normal(k2, (B, F, D), dtype=jnp.float32)
        return {'dense_features': dense_features, 'sparse_values': sparse_values}
    _L0_rec_all = _L0_rec_setup()
    _L0_rec_in = {k: v for k, v in _L0_rec_all.items() if k in ()}
    del _L0_rec_all
    return {'r_dense_features': r_dense_features, 'ids': ids, 'tbl_0': tbl_0, 'tbl_1': tbl_1, 'tbl_2': tbl_2, 'tbl_3': tbl_3, 'tbl_4': tbl_4, 'tbl_5': tbl_5, 'tbl_6': tbl_6, 'tbl_7': tbl_7, 'tbl_8': tbl_8, 'tbl_9': tbl_9, 'tbl_10': tbl_10, 'tbl_11': tbl_11, 'tbl_12': tbl_12, 'tbl_13': tbl_13, 'tbl_14': tbl_14, 'tbl_15': tbl_15, 'tbl_16': tbl_16, 'tbl_17': tbl_17, 'tbl_18': tbl_18, 'tbl_19': tbl_19, 'tbl_20': tbl_20, 'tbl_21': tbl_21, 'tbl_22': tbl_22, 'tbl_23': tbl_23, 'tbl_24': tbl_24, 'tbl_25': tbl_25, 'W_top1': W_top1, 'b_top1': b_top1, 'W_top2': W_top2, 'b_top2': b_top2, 'W_top3': W_top3}

def reference(r_dense_features, ids, tbl_0, tbl_1, tbl_2, tbl_3, tbl_4, tbl_5, tbl_6, tbl_7, tbl_8, tbl_9, tbl_10, tbl_11, tbl_12, tbl_13, tbl_14, tbl_15, tbl_16, tbl_17, tbl_18, tbl_19, tbl_20, tbl_21, tbl_22, tbl_23, tbl_24, tbl_25, W_top1, b_top1, W_top2, b_top2, W_top3):
    import jax
    import jax.numpy as jnp

    def _L0_rec_ref(dense_features, sparse_values):
        import jax, jax.numpy as jnp
        import numpy as np
        B, F, D = (2048, 26, 128)
        sd = jnp.einsum('bfd,bd->bf', sparse_values, dense_features)
        ss = jnp.einsum('bfd,bgd->bfg', sparse_values, sparse_values)
        iu, ju = jnp.triu_indices(F, k=1)
        pairs = ss[:, iu, ju]
        return jnp.concatenate([dense_features, sd, pairs], axis=1)
    e = jnp.stack([tbl_0[ids[:, 0]], tbl_1[ids[:, 1]], tbl_2[ids[:, 2]], tbl_3[ids[:, 3]], tbl_4[ids[:, 4]], tbl_5[ids[:, 5]], tbl_6[ids[:, 6]], tbl_7[ids[:, 7]], tbl_8[ids[:, 8]], tbl_9[ids[:, 9]], tbl_10[ids[:, 10]], tbl_11[ids[:, 11]], tbl_12[ids[:, 12]], tbl_13[ids[:, 13]], tbl_14[ids[:, 14]], tbl_15[ids[:, 15]], tbl_16[ids[:, 16]], tbl_17[ids[:, 17]], tbl_18[ids[:, 18]], tbl_19[ids[:, 19]], tbl_20[ids[:, 20]], tbl_21[ids[:, 21]], tbl_22[ids[:, 22]], tbl_23[ids[:, 23]], tbl_24[ids[:, 24]], tbl_25[ids[:, 25]]], axis=1)
    z = _L0_rec_ref(r_dense_features, e)
    z = z.reshape(z.shape[0], -1)
    h = jnp.concatenate([z, r_dense_features], axis=1)
    h = jnp.maximum(h @ W_top1 + b_top1, 0.0)
    h = jnp.maximum(h @ W_top2 + b_top2, 0.0)
    y = h @ W_top3
    return y

_drawn_inputs = setup_inputs


def setup_inputs(seed=0):
    import zlib

    import numpy as np

    out = dict(_drawn_inputs(seed))
    spreads = {'b_top1': (0.0, 0.1), 'b_top2': (0.0, 0.1)}
    factors = {}
    for name, (base, spread) in spreads.items():
        noise = np.random.default_rng([zlib.crc32(name.encode()), seed]).standard_normal(out[name].shape)
        drawn = base * np.exp(spread * noise) if base else spread * noise
        out[name] = jnp.asarray(drawn.astype(out[name].dtype))
    for name, factor in factors.items():
        out[name] = (out[name] * factor).astype(out[name].dtype)
    return out
```

```python
from contextlib import ExitStack

import concourse.bass as bass
from concourse import mybir

F32 = mybir.dt.float32
I32 = mybir.dt.int32
ALU = mybir.AluOpType
ACT = mybir.ActivationFunctionType

P = 128
TABLES = 26
FEATURES = TABLES + 1
PAIRS = FEATURES * (FEATURES - 1) // 2
SLOT = 32
BANK = 512

TILES = 4
CHUNK = TILES * P
GROUP = P // SLOT
GROUPS = P // GROUP
WIDE = GROUP * FEATURES

TURN = BANK // P
TURNS = -(-FEATURES // TURN)
UNIT_BANKS = 2
PER_BANK = BANK // WIDE
UNIT = UNIT_BANKS * PER_BANK
UNITS = GROUPS // UNIT

K_PAIRS = 3
PK = PAIRS // K_PAIRS
COLS_TURNS = -(-TABLES // TURN)
DMA = 16


def offset(row):
    return row * FEATURES - row * (row + 1) // 2


def dlrm_tower(nc, dense, ids, tables, w1, b1, w2, b2, w3, out):
    B, D = dense.shape
    H1, H2 = w1.shape[1], w2.shape[1]
    N1, N2 = H1 // P, H2 // P
    chunks = B // CHUNK
    assert D == P and PK * K_PAIRS == PAIRS and B % CHUNK == 0
    first_pair, dense_again = D, D + PAIRS

    with ExitStack() as ctx:
        def sb(name, shape, dt=F32):
            return ctx.enter_context(nc.sbuf_tensor(name, shape, dt))

        def sem(name):
            return ctx.enter_context(nc.semaphore(name))

        ident = sb("ident", [P, P])
        w1_dense = sb("w1_dense", [P, H1])
        w1_again = sb("w1_again", [P, H1])
        w1_pairs = sb("w1_pairs", [PK, K_PAIRS, H1])
        w2_sb = sb("w2_sb", [P, N1, H2])
        w3_sb = sb("w3_sb", [P, N2])
        b1_sb = sb("b1_sb", [P, N1])
        b2_sb = sb("b2_sb", [P, N2])

        index = sb("index", [P, TILES, TABLES], I32)
        rows = sb("rows", [P, TILES, FEATURES, D])
        turned = sb("turned", [P, 2, GROUPS, GROUP * SLOT])
        dense_t = sb("dense_t", [P, CHUNK])
        gram = sb("gram", [P, TILES * GROUPS, FEATURES])
        pairs = sb("pairs", [P, GROUP, PAIRS])
        pairs_t = sb("pairs_t", [PK, K_PAIRS, CHUNK])
        h1 = sb("h1", [P, N1, CHUNK])
        h2 = sb("h2", [P, N2, CHUNK])
        y = sb("y", [1, B])

        turn_bank = [ctx.enter_context(nc.psum_tensor(f"turn_bank{i}", [P, TURN, P], F32)) for i in range(2)]
        gram_bank = [ctx.enter_context(nc.psum_tensor(f"gram_bank{i}", [P, UNIT_BANKS, BANK], F32)) for i in range(2)]
        late_bank = [ctx.enter_context(nc.psum_tensor(f"late_bank{i}", [P, BANK], F32)) for i in range(2)]

        ident_made = sem("ident_made")
        weights_loaded = sem("weights_loaded")
        padded = sem("padded")
        w1_merged = sem("w1_merged")
        index_loaded = [sem(f"index_loaded{t}") for t in range(TILES)]
        dense_loaded = [sem(f"dense_loaded{t}") for t in range(TILES)]
        gathered = [sem(f"gathered{t}") for t in range(TILES)]
        gathers_begun = sem("gathers_begun")
        rows_turned = sem("rows_turned")
        rows_copied = sem("rows_copied")
        gram_done = sem("gram_done")
        gram_copied = sem("gram_copied")
        cols_turned = sem("cols_turned")
        cols_copied = sem("cols_copied")
        pairs_turned = sem("pairs_turned")
        pairs_copied = sem("pairs_copied")
        h1_summed = sem("h1_summed")
        h1_made = sem("h1_made")
        h2_summed = sem("h2_summed")
        h2_made = sem("h2_made")
        y_summed = sem("y_summed")
        y_copied = sem("y_copied")
        stored = sem("stored")

        w1_rows = w1[first_pair:first_pair + PAIRS, :].rearrange("(k p) n -> p k n", p=PK)
        weight_loads = [
            (w1_dense[:], w1[0:D, :]),
            (w1_again[:], w1[dense_again:dense_again + D, :]),
            (w1_pairs[:], w1_rows),
            (w2_sb[:], w2.rearrange("(k p) n -> p k n", p=P)),
            (w3_sb[:], w3),
            (b1_sb[:], b1),
            (b2_sb[:], b2),
        ]
        ids_t = ids.rearrange("(n p) f -> n p f", p=P)
        dense_tiles = dense.rearrange("(n p) d -> n p d", p=P)

        block = ctx.enter_context(nc.Block())

        @block.sync
        def _(sp):
            with sp.Fori(0, chunks) as c:
                for t in range(TILES):
                    sp.wait_ge(rows_copied, c * (TILES * TURNS) + (t + 1) * TURNS)
                    sp.dma_start(index[:, t, :], ids_t[bass.ds(c * TILES + t, 1), :, :].rearrange("n p f -> p (n f)")).then_inc(index_loaded[t], DMA)
                    sp.dma_start(rows[:, t, 0, :], dense_tiles[bass.ds(c * TILES + t, 1), :, :].rearrange("n p d -> p (n d)")).then_inc(dense_loaded[t], DMA)

        @block.gpsimd
        def _(pool):
            pool.memset(ident[:], 0.0).then_inc(ident_made, 1)
            pool.wait_ge(ident_made, 1)
            pool.affine_select(out=ident[:], in_=ident[:], compare_op=ALU.not_equal, fill=1.0, base=0,
                               pattern=[[-1, P]], channel_multiplier=1).then_inc(ident_made, 1)
            with pool.Fori(0, chunks) as c:
                for t in range(TILES):
                    pool.wait_ge(index_loaded[t], (c + 1) * DMA)
                    pool.sem_inc(gathers_begun, 1)
                    for f in range(TABLES):
                        pool.indirect_dma_start(
                            out=rows[:, t, f + 1, :], out_offset=None, in_=tables[f],
                            in_offset=bass.IndirectOffsetOnAxis(ap=index[:, t, f:f + 1], axis=0),
                        ).then_inc(gathered[t], DMA)

        @block.tensor
        def _(pe):
            def turn_rows(c, t):
                pe.wait_ge(dense_loaded[t], (c + 1) * DMA)
                pe.wait_ge(gathered[t], (c + 1) * (TABLES * DMA))
                for g in range(TURNS):
                    n = t * TURNS + g
                    pe.wait_ge(rows_copied, (c + 1) * (TILES * TURNS) + n - 1)
                    for f in range(g * TURN, min((g + 1) * TURN, FEATURES)):
                        last = pe.transpose(turn_bank[n % 2][:, f % TURN, :], rows[:, t, f, :], ident[:])
                    last.then_inc(rows_turned, 1)

            def products(c, t):
                pe.wait_ge(rows_copied, (c + 1) * (TILES * TURNS) + (t + 1) * TURNS)
                for u in range(UNITS):
                    n = t * UNITS + u
                    pe.wait_ge(gram_copied, (c + 1) * (TILES * UNITS) + n - 1)
                    for k in range(UNIT):
                        bank, col = k // PER_BANK, k % PER_BANK * WIDE
                        group = turned[:, t % 2, u * UNIT + k]
                        last = pe.matmul(gram_bank[n % 2][:, bank, col:col + WIDE], group,
                                         group.rearrange("p (q f) -> p q f", q=GROUP)[:, :, 0:FEATURES],
                                         start=True, stop=True)
                    last.then_inc(gram_done, 1)

            def turn_pairs(c):
                pe.wait_ge(gram_copied, (c + 2) * (TILES * UNITS))
                for g in range(COLS_TURNS):
                    if g == 0:
                        pe.wait_ge(y_copied, c + 1)
                    elif g == 1:
                        pe.wait_ge(h2_made, (c + 1) * N2)
                    else:
                        pe.wait_ge(cols_copied, (c + 1) * COLS_TURNS + g - 1)
                    for i in range(g * TURN, min((g + 1) * TURN, TABLES)):
                        last = pe.transpose(late_bank[g % 2][:, i % TURN * P:(i % TURN + 1) * P], gram[:, :, i], ident[:])
                    last.then_inc(cols_turned, 1)
                pe.wait_ge(cols_copied, (c + 2) * COLS_TURNS)
                for k in range(K_PAIRS):
                    if k == 2:
                        pe.wait_ge(pairs_copied, (c + 1) * K_PAIRS + 1)
                    to = late_bank[(COLS_TURNS + k) % 2][0:PK, :].rearrange("p (t q i) -> p q t i", t=TILES, q=GROUP)
                    for q in range(GROUP):
                        last = pe.transpose(to[:, q], pairs[:, q, k * PK:(k + 1) * PK], ident[:])
                    last.then_inc(pairs_turned, 1)

            def mlp(c):
                at = COLS_TURNS + K_PAIRS
                pe.wait_ge(pairs_copied, (c + 2) * K_PAIRS)
                for n in range(N1):
                    if n >= 2:
                        pe.wait_ge(h1_made, (c + 1) * N1 + n - 1)
                    to = late_bank[(at + n) % 2][:]
                    cols = slice(n * P, (n + 1) * P)
                    pe.matmul(to, w1_dense[:, cols], dense_t[:], start=True, stop=False)
                    for k in range(K_PAIRS):
                        last = pe.matmul(to, w1_pairs[:, k, cols], pairs_t[:, k, :], start=False, stop=k == K_PAIRS - 1)
                    last.then_inc(h1_summed, 1)
                at += N1
                pe.wait_ge(h1_made, (c + 2) * N1)
                for n in range(N2):
                    to = late_bank[(at + n) % 2][:]
                    for k in range(N1):
                        last = pe.matmul(to, w2_sb[:, k, n * P:(n + 1) * P], h1[:, k, :], start=k == 0, stop=k == N1 - 1)
                    last.then_inc(h2_summed, 1)
                at += N2
                pe.wait_ge(h2_made, (c + 2) * N2)
                for k in range(N2):
                    last = pe.matmul(late_bank[at % 2][0:1, :], w3_sb[:, k:k + 1], h2[:, k, :], start=k == 0, stop=k == N2 - 1)
                last.then_inc(y_summed, 1)

            pe.wait_ge(ident_made, 2)
            pe.wait_ge(weights_loaded, len(weight_loads) * DMA)
            pe.wait_ge(w1_merged, 1)
            with pe.Fori(0, chunks) as c:
                for t in range(TILES):
                    turn_rows(c, t)
                    products(c, t)
                turn_pairs(c)
                mlp(c)

        @block.scalar
        def _(act):
            act.sem_inc(rows_copied, TILES * TURNS)
            act.sem_inc(pairs_copied, K_PAIRS)
            act.sem_inc(h1_made, N1)
            act.sem_inc(h2_made, N2)
            act.sem_inc(y_copied, 1)
            for to, of in weight_loads:
                act.dma_start(to, of).then_inc(weights_loaded, DMA)
            act.wait_ge(padded, 1)
            with act.Fori(0, chunks) as c:
                for t in range(TILES):
                    tile = turned[:, t % 2].rearrange("p i (q f) -> p f q i", q=GROUP)
                    for g in range(TURNS):
                        n = t * TURNS + g
                        act.wait_ge(rows_turned, c * (TILES * TURNS) + n + 1)
                        if g == 0:
                            nc.scalar.copy(dense_t[:, t * P:(t + 1) * P], turn_bank[n % 2][:, 0, :])
                        f0, f1 = g * TURN, min((g + 1) * TURN, FEATURES)
                        of = turn_bank[n % 2][:, 0:f1 - f0, :].rearrange("p f (q i) -> p f q i", q=GROUP)
                        nc.scalar.copy(tile[:, f0:f1], of).then_inc(rows_copied, 1)
                for k in range(K_PAIRS):
                    act.wait_ge(pairs_turned, c * K_PAIRS + k + 1)
                    nc.scalar.copy(pairs_t[:, k, :], late_bank[(COLS_TURNS + k) % 2][0:PK, :]).then_inc(pairs_copied, 1)
                at = COLS_TURNS + K_PAIRS
                for n in range(N1):
                    act.wait_ge(h1_summed, c * N1 + n + 1)
                    nc.scalar.activation(h1[:, n, :], late_bank[(at + n) % 2][:], ACT.Relu,
                                         bias=b1_sb[:, n:n + 1]).then_inc(h1_made, 1)
                at += N1
                for n in range(N2):
                    act.wait_ge(h2_summed, c * N2 + n + 1)
                    nc.scalar.activation(h2[:, n, :], late_bank[(at + n) % 2][:], ACT.Relu,
                                         bias=b2_sb[:, n:n + 1]).then_inc(h2_made, 1)
                at += N2
                act.wait_ge(y_summed, c + 1)
                nc.scalar.copy(y[:, bass.ds(c * CHUNK, CHUNK)], late_bank[at % 2][0:1, :]).then_inc(y_copied, 1)
            act.wait_ge(y_copied, chunks + 1)
            act.dma_start(out.rearrange("b n -> n b"), y[:]).then_inc(stored, DMA)
            act.wait_ge(stored, DMA)

        @block.vector
        def _(dve):
            dve.sem_inc(gram_copied, TILES * UNITS)
            dve.sem_inc(cols_copied, COLS_TURNS)
            dve.memset(turned[:], 0.0).then_inc(padded, 1)
            dve.wait_ge(weights_loaded, len(weight_loads) * DMA)
            dve.tensor_tensor(w1_dense[:], w1_dense[:], w1_again[:], ALU.add).then_inc(w1_merged, 1)
            with dve.Fori(0, chunks) as c:
                for n in range(TILES * UNITS):
                    dve.wait_ge(gram_done, c * (TILES * UNITS) + n + 1)
                    for q in range(GROUP):
                        part = slice(q * SLOT, (q + 1) * SLOT)
                        of = gram_bank[n % 2][part, :, 0:PER_BANK * WIDE].rearrange(
                            "p b (k q f) -> p b k q f", k=PER_BANK, q=GROUP)[:, :, :, q]
                        to = gram[part, n * UNIT:(n + 1) * UNIT, :].rearrange("p (b k) f -> p b k f", b=UNIT_BANKS)
                        last = nc.vector.tensor_copy(to, of)
                    last.then_inc(gram_copied, 1)
                for g in range(COLS_TURNS):
                    dve.wait_ge(cols_turned, c * COLS_TURNS + g + 1)
                    for i in range(g * TURN, min((g + 1) * TURN, TABLES)):
                        of = late_bank[g % 2][:, i % TURN * P:(i % TURN + 1) * P].rearrange("p (q f) -> p q f", q=GROUP)
                        last = nc.vector.tensor_copy(pairs[:, :, offset(i):offset(i + 1)], of[:, :, i + 1:FEATURES])
                    last.then_inc(cols_copied, 1)


_TABLES = [f"tbl_{i}" for i in range(TABLES)]
_INS = ["r_dense_features", "ids", *_TABLES, "W_top1", "b_top1", "W_top2", "b_top2", "W_top3"]
_BY_PARTITION = ("b_top1", "b_top2", "W_top3")


def kernel(**inputs):
    import numpy as _np
    import concourse.bacc as _bacc
    from concourse import mybir as _mybir
    from concourse.bass_utils import run_bass_kernel_spmd as _run

    nc = _bacc.Bacc("TRN2", target_bir_lowering=False, num_devices=1)
    arrays, args = {}, {}
    for name in _INS:
        a = _np.ascontiguousarray(inputs[name])
        if name in _BY_PARTITION:
            a = _np.ascontiguousarray(a.reshape(-1, P).T)
        arrays[f"in_{name}_dram"] = a
        args[name] = nc.dram_tensor(f"in_{name}_dram", a.shape, _mybir.dt.from_np(a.dtype), kind="ExternalInput").ap()
    shape = (inputs["r_dense_features"].shape[0], 1)
    out = nc.dram_tensor("out_0_dram", shape, F32, kind="ExternalOutput").ap()
    dlrm_tower(nc, args["r_dense_features"], args["ids"], [args[n] for n in _TABLES], args["W_top1"],
               args["b_top1"], args["W_top2"], args["b_top2"], args["W_top3"], out)
    r = _run(nc, [arrays], core_ids=[0])
    return r.results[0]["out_0_dram"]
```

```python
from contextlib import ExitStack

import concourse.bass as bass
from concourse import mybir

F32 = mybir.dt.float32
F32R = mybir.dt.float32r
I32 = mybir.dt.int32
ALU = mybir.AluOpType
ACT = mybir.ActivationFunctionType

P = 128
LOOKED_UP = (6, 9, 15, 16, 17, 18, 20)
GATHERED = tuple(f for f in range(26) if f not in LOOKED_UP)
FEATURES = 1 + len(GATHERED) + len(LOOKED_UP)
ROWS = 1 + len(GATHERED)
LOOKUPS = len(LOOKED_UP)
PAIRS = FEATURES * (FEATURES - 1) // 2
SLOT = 32
BANK = 512

TILES = 4
CHUNK = TILES * P
GROUP = P // SLOT
GROUPS = P // GROUP
WIDE = GROUP * FEATURES
TALL = (GROUP - 1) * SLOT + FEATURES

TURN = BANK // P
TURNS = -(-ROWS // TURN)
UNIT_BANKS = 2
PER_BANK = BANK // WIDE
UNIT = UNIT_BANKS * PER_BANK
UNITS = GROUPS // UNIT
COLS_TURNS = -(-(FEATURES - 1) // TURN)

K_PAIRS = 3
PK = PAIRS // K_PAIRS
K_ROWS = 8
HOT_SLOTS = 4
ID_SLOTS = 4
DMA = 16


def offset(row):
    return row * FEATURES - row * (row + 1) // 2


def turn_range(g):
    return g * TURN, min((g + 1) * TURN, ROWS)


def dlrm_tower(nc, dense, ids, ids_t, tables, w1, b1, w2, b2, w3, out):
    B, D = dense.shape
    H1, H2 = w1.shape[1], w2.shape[1]
    N1, N2 = H1 // P, H2 // P
    chunks = B // CHUNK
    RK = tables[LOOKED_UP[0]].shape[0] // K_ROWS
    assert D == P and PK * K_PAIRS == PAIRS and B % CHUNK == 0
    assert all(tables[f].shape[0] == RK * K_ROWS for f in LOOKED_UP) and K_ROWS % HOT_SLOTS == 0
    first_pair, dense_again = D, D + PAIRS
    ALL_TURNS, ALL_UNITS, HOTS = TILES * TURNS, TILES * UNITS, LOOKUPS * K_ROWS

    with ExitStack() as ctx:
        def sb(name, shape, dt=F32):
            return ctx.enter_context(nc.sbuf_tensor(name, shape, dt))

        def sem(name):
            return ctx.enter_context(nc.semaphore(name))

        ident = sb("ident", [P, P])
        w1_dense = sb("w1_dense", [P, H1])
        w1_pairs = sb("w1_pairs", [PK, K_PAIRS, H1])
        w2_sb = sb("w2_sb", [P, N1, H2])
        w3_sb = sb("w3_sb", [P, N2])
        b1_sb = sb("b1_sb", [P, N1])
        b2_sb = sb("b2_sb", [P, N2])
        table_hi = sb("table_hi", [RK, LOOKUPS, K_ROWS, D], F32R)
        table_lo = sb("table_lo", [RK, LOOKUPS, K_ROWS, D], F32R)
        row_number = sb("row_number", [RK, K_ROWS])
        row_number_int = sb("row_number_int", [RK, K_ROWS], I32)

        index = sb("index", [P, TILES, 26], I32)
        rows = sb("rows", [P, TILES, ROWS, D])
        turned = sb("turned", [P, 2, GROUPS, GROUP * SLOT])
        table_ids = sb("table_ids", [RK, ID_SLOTS, CHUNK], I32)
        one_hot = sb("one_hot", [RK, HOT_SLOTS, CHUNK], F32R)
        looked_up = sb("looked_up", [P, LOOKUPS, CHUNK])
        dense_t = sb("dense_t", [P, CHUNK])
        gram = sb("gram", [P, TILES * GROUPS, FEATURES])
        pairs = sb("pairs", [P, GROUP, PAIRS])
        pairs_t = sb("pairs_t", [PK, K_PAIRS, CHUNK])
        h1 = sb("h1", [P, N1, CHUNK])
        h2 = sb("h2", [P, N2, CHUNK])
        y = sb("y", [1, CHUNK])
        raw = turned[:].rearrange("p a i f -> p (a i f)")[0:RK, 0:LOOKUPS * K_ROWS * D].rearrange(
            "p (s n) -> p s n", s=LOOKUPS)
        w1_again = gram[:].rearrange("p a f -> p (a f)")[:, 0:H1]

        turn_bank = [ctx.enter_context(nc.psum_tensor(f"turn_bank{i}", [P, TURN, P], F32)) for i in range(2)]
        gram_bank = [ctx.enter_context(nc.psum_tensor(f"gram_bank{i}", [P, UNIT_BANKS, BANK], F32)) for i in range(2)]
        late_bank = [ctx.enter_context(nc.psum_tensor(f"late_bank{i}", [P, BANK], F32)) for i in range(2)]

        ident_made = sem("ident_made")
        numbers_made = sem("numbers_made")
        numbers_ready = sem("numbers_ready")
        weights_loaded = sem("weights_loaded")
        table_loaded = [sem(f"table_loaded{s}") for s in range(LOOKUPS)]
        hi_made = sem("hi_made")
        lo_made = sem("lo_made")
        padded = sem("padded")
        w1_merged = sem("w1_merged")
        index_loaded = [sem(f"index_loaded{t}") for t in range(TILES)]
        dense_loaded = [sem(f"dense_loaded{t}") for t in range(TILES)]
        ids_loaded = [sem(f"ids_loaded{s}") for s in range(LOOKUPS)]
        gathers_begun = sem("gathers_begun")
        gathered = [[sem(f"gathered{t}_{g}") for g in range(TURNS)] for t in range(TILES)]
        one_hot_made = sem("one_hot_made")
        one_hot_used = sem("one_hot_used")
        rows_found = sem("rows_found")
        found_copied = sem("found_copied")
        found_placed = sem("found_placed")
        rows_turned = sem("rows_turned")
        rows_copied = sem("rows_copied")
        gram_done = sem("gram_done")
        gram_copied = sem("gram_copied")
        cols_turned = sem("cols_turned")
        cols_copied = sem("cols_copied")
        pairs_turned = sem("pairs_turned")
        pairs_copied = sem("pairs_copied")
        h1_summed = sem("h1_summed")
        h1_made = sem("h1_made")
        h2_summed = sem("h2_summed")
        h2_made = sem("h2_made")
        y_summed = sem("y_summed")
        y_copied = sem("y_copied")
        stored = sem("stored")

        w1_rows = w1[first_pair:first_pair + PAIRS, :].rearrange("(k p) n -> p k n", p=PK)
        weight_loads = [
            (w1_dense[:], w1[0:D, :]),
            (w1_again, w1[dense_again:dense_again + D, :]),
            (w1_pairs[:], w1_rows),
            (w2_sb[:], w2.rearrange("(k p) n -> p k n", p=P)),
            (w3_sb[:], w3),
            (b1_sb[:], b1),
            (b2_sb[:], b2),
        ]
        index_tiles = ids.rearrange("(n p) f -> n p f", p=P)
        dense_tiles = dense.rearrange("(n p) d -> n p d", p=P)
        PAIRS_AT = COLS_TURNS
        H1_AT = PAIRS_AT + K_PAIRS
        H2_AT = H1_AT + N1
        Y_AT = H2_AT + N2

        block = ctx.enter_context(nc.Block())

        @block.sync
        def _(sp):
            def load_tile(c, t):
                sp.wait_ge(rows_copied, c * ALL_TURNS + (t + 1) * TURNS)
                of = bass.ds(c * TILES + t, 1)
                sp.dma_start(index[:, t, :], index_tiles[of].rearrange("n p f -> p (n f)")).then_inc(index_loaded[t], DMA)
                sp.dma_start(rows[:, t, 0, :], dense_tiles[of].rearrange("n p d -> p (n d)")).then_inc(dense_loaded[t], DMA)

            with sp.Fori(0, chunks) as c:
                for t in range(TILES):
                    load_tile(c, t)

        @block.gpsimd
        def _(pool):
            pool.memset(ident[:], 0.0).then_inc(ident_made, 1)
            pool.iota(row_number_int[:], pattern=[[1, K_ROWS]], base=0, channel_multiplier=K_ROWS).then_inc(numbers_made, 1)
            pool.wait_ge(ident_made, 1)
            pool.affine_select(out=ident[:], in_=ident[:], compare_op=ALU.not_equal, fill=1.0, base=0,
                               pattern=[[-1, P]], channel_multiplier=1).then_inc(ident_made, 1)
            with pool.Fori(0, chunks) as c:
                for t in range(TILES):
                    pool.wait_ge(index_loaded[t], (c + 1) * DMA)
                    pool.sem_inc(gathers_begun, 1)
                    for n, f in enumerate(GATHERED):
                        pool.indirect_dma_start(
                            out=rows[:, t, n + 1, :], out_offset=None, in_=tables[f],
                            in_offset=bass.IndirectOffsetOnAxis(ap=index[:, t, f:f + 1], axis=0),
                        ).then_inc(gathered[t][(n + 1) // TURN], DMA)

        @block.tensor
        def _(pe):
            def look_up(c, s):
                if s >= 2:
                    pe.wait_ge(found_copied, (c + 1) * LOOKUPS + s - 1)
                bank = turn_bank[s % 2][:].rearrange("p f b -> p (f b)")
                for k in range(K_ROWS):
                    n = s * K_ROWS + k
                    pe.wait_ge(one_hot_made, c * HOTS + n + 1)
                    hot = one_hot[:, n % HOT_SLOTS, :]
                    pe.matmul(bank, table_hi[:, s, k, :], hot, start=k == 0, stop=False)
                    pe.matmul(bank, table_lo[:, s, k, :], hot, start=False, stop=k == K_ROWS - 1).then_inc(one_hot_used, 1)

            def turn_rows(c, t, g):
                n = t * TURNS + g
                if g == 0:
                    pe.wait_ge(dense_loaded[t], (c + 1) * DMA)
                f0, f1 = turn_range(g)
                pe.wait_ge(gathered[t][g], (c + 1) * DMA * (f1 - f0 - (g == 0)))
                if n < 2:
                    pe.wait_ge(found_copied, (c + 2) * LOOKUPS)
                else:
                    pe.wait_ge(rows_copied, (c + 1) * ALL_TURNS + n - 1)
                for f in range(f0, f1):
                    last = pe.transpose(turn_bank[n % 2][:, f - f0, :], rows[:, t, f, :], ident[:])
                last.then_inc(rows_turned, 1)

            def products(c, t, u):
                if u == 0:
                    pe.wait_ge(rows_copied, (c + 1) * ALL_TURNS + (t + 1) * TURNS)
                    pe.wait_ge(found_placed, c * TILES + t + 1)
                n = t * UNITS + u
                pe.wait_ge(gram_copied, (c + 1) * ALL_UNITS + n - 1)
                for k in range(UNIT):
                    bank, col = k // PER_BANK, k % PER_BANK * WIDE
                    group = turned[:, t % 2, u * UNIT + k]
                    last = pe.matmul(gram_bank[n % 2][0:TALL, bank, col:col + WIDE], group[:, 0:TALL],
                                     group.rearrange("p (q f) -> p q f", q=GROUP)[:, :, 0:FEATURES],
                                     start=True, stop=True)
                last.then_inc(gram_done, 1)

            def turn_products(c):
                pe.wait_ge(gram_copied, (c + 2) * ALL_UNITS)
                for g in range(COLS_TURNS):
                    if g == 0:
                        pe.wait_ge(y_copied, c + 1)
                    elif g == 1:
                        pe.wait_ge(h2_made, (c + 1) * N2)
                    else:
                        pe.wait_ge(cols_copied, (c + 1) * COLS_TURNS + g - 1)
                    for i in range(g * TURN, min((g + 1) * TURN, FEATURES - 1)):
                        last = pe.transpose(late_bank[g % 2][:, i % TURN * P:i % TURN * P + TALL],
                                            gram[0:TALL, :, i], ident[0:TALL, 0:TALL])
                    last.then_inc(cols_turned, 1)

            def turn_pairs(c):
                pe.wait_ge(cols_copied, (c + 2) * COLS_TURNS)
                for k in range(K_PAIRS):
                    if k == 2:
                        pe.wait_ge(pairs_copied, (c + 1) * K_PAIRS + 1)
                    to = late_bank[(PAIRS_AT + k) % 2][0:PK, :].rearrange("p (t q i) -> p q t i", t=TILES, q=GROUP)
                    for q in range(GROUP):
                        last = pe.transpose(to[:, q], pairs[:, q, k * PK:(k + 1) * PK], ident[:])
                    last.then_inc(pairs_turned, 1)

            def layer1(c, n):
                if n == 0:
                    pe.wait_ge(pairs_copied, (c + 2) * K_PAIRS)
                elif n >= 2:
                    pe.wait_ge(h1_made, (c + 1) * N1 + n - 1)
                to = late_bank[(H1_AT + n) % 2][:]
                cols = slice(n * P, (n + 1) * P)
                pe.matmul(to, w1_dense[:, cols], dense_t[:], start=True, stop=False)
                for k in range(K_PAIRS):
                    last = pe.matmul(to, w1_pairs[:, k, cols], pairs_t[:, k, :], start=False, stop=k == K_PAIRS - 1)
                last.then_inc(h1_summed, 1)

            def layer2(c, n):
                if n == 0:
                    pe.wait_ge(h1_made, (c + 2) * N1)
                to = late_bank[(H2_AT + n) % 2][:]
                for k in range(N1):
                    last = pe.matmul(to, w2_sb[:, k, n * P:(n + 1) * P], h1[:, k, :], start=k == 0, stop=k == N1 - 1)
                last.then_inc(h2_summed, 1)

            def layer3(c):
                pe.wait_ge(h2_made, (c + 2) * N2)
                for k in range(N2):
                    last = pe.matmul(late_bank[Y_AT % 2][0:1, :], w3_sb[:, k:k + 1], h2[:, k, :], start=k == 0, stop=k == N2 - 1)
                last.then_inc(y_summed, 1)

            def tiles(c):
                for g in range(TURNS):
                    turn_rows(c, 0, g)
                for t in range(TILES):
                    if t + 1 < TILES:
                        turn_rows(c, t + 1, 0)
                    for u in range(UNITS):
                        if t + 1 < TILES and u + 1 < TURNS:
                            turn_rows(c, t + 1, u + 1)
                        products(c, t, u)

            pe.wait_ge(ident_made, 2)
            for s in range(LOOKUPS):
                pe.wait_ge(lo_made, s + 1)
                look_up(0, s)
            pe.wait_ge(weights_loaded, len(weight_loads) * DMA)
            pe.wait_ge(w1_merged, 1)
            with pe.Fori(0, chunks - 1) as c:
                tiles(c)
                turn_products(c)
                look_up(c + 1, 0)
                turn_pairs(c)
                look_up(c + 1, 1)
                for n in range(N1):
                    layer1(c, n)
                look_up(c + 1, 2)
                for n in range(N2):
                    layer2(c, n)
                look_up(c + 1, 3)
                layer3(c)
                for s in range(4, LOOKUPS):
                    look_up(c + 1, s)
            tiles(chunks - 1)
            turn_products(chunks - 1)
            turn_pairs(chunks - 1)
            for n in range(N1):
                layer1(chunks - 1, n)
            for n in range(N2):
                layer2(chunks - 1, n)
            layer3(chunks - 1)

        @block.scalar
        def _(act):
            def load_ids(c, s):
                act.dma_start(table_ids[:, s % ID_SLOTS, :],
                              ids_t[LOOKED_UP[s], bass.ds(c * CHUNK, CHUNK)].partition_broadcast(RK)).then_inc(ids_loaded[s], DMA)

            def load_next_ids(c, s):
                act.wait_ge(one_hot_made, c * HOTS + (s + 1) * K_ROWS)
                load_ids(c, s + ID_SLOTS)

            def copy_found(c, s):
                act.wait_ge(one_hot_used, (c + 1) * HOTS + (s + 1) * K_ROWS)
                nc.scalar.copy(looked_up[:, s, :], turn_bank[s % 2][:].rearrange("p f b -> p (f b)")).then_inc(found_copied, 1)
                if s + ID_SLOTS < LOOKUPS:
                    load_next_ids(c, s)

            def copy_rows(c, t, g):
                n = t * TURNS + g
                act.wait_ge(rows_turned, c * ALL_TURNS + n + 1)
                if g == 0:
                    nc.scalar.copy(dense_t[:, t * P:(t + 1) * P], turn_bank[n % 2][:, 0, :])
                f0, f1 = turn_range(g)
                to = turned[:, t % 2].rearrange("p i (q f) -> p f q i", q=GROUP)
                of = turn_bank[n % 2][:, 0:f1 - f0, :].rearrange("p f (q i) -> p f q i", q=GROUP)
                nc.scalar.copy(to[:, f0:f1], of).then_inc(rows_copied, 1)

            def copy_pairs(c):
                for k in range(K_PAIRS):
                    act.wait_ge(pairs_turned, c * K_PAIRS + k + 1)
                    nc.scalar.copy(pairs_t[:, k, :], late_bank[(PAIRS_AT + k) % 2][0:PK, :]).then_inc(pairs_copied, 1)

            def relu1(c):
                for n in range(N1):
                    act.wait_ge(h1_summed, c * N1 + n + 1)
                    nc.scalar.activation(h1[:, n, :], late_bank[(H1_AT + n) % 2][:], ACT.Relu,
                                         bias=b1_sb[:, n:n + 1]).then_inc(h1_made, 1)

            def relu2(c):
                for n in range(N2):
                    act.wait_ge(h2_summed, c * N2 + n + 1)
                    nc.scalar.activation(h2[:, n, :], late_bank[(H2_AT + n) % 2][:], ACT.Relu,
                                         bias=b2_sb[:, n:n + 1]).then_inc(h2_made, 1)

            def output(c):
                act.wait_ge(y_summed, c + 1)
                nc.scalar.copy(y[:], late_bank[Y_AT % 2][0:1, :]).then_inc(y_copied, 1)
                act.wait_ge(y_copied, c + 2)
                act.dma_start(out[bass.ds(c * CHUNK, CHUNK), :].rearrange("b n -> n b"), y[:]).then_inc(stored, DMA)

            act.sem_inc(rows_copied, ALL_TURNS)
            act.sem_inc(found_copied, LOOKUPS)
            act.sem_inc(pairs_copied, K_PAIRS)
            act.sem_inc(h1_made, N1)
            act.sem_inc(h2_made, N2)
            act.sem_inc(y_copied, 1)
            for s in range(LOOKUPS):
                act.dma_start(raw[:, s, :], tables[LOOKED_UP[s]].rearrange("(p k) d -> p (k d)", k=K_ROWS)).then_inc(table_loaded[s], DMA)
                if s < ID_SLOTS:
                    load_ids(0, s)
            for to, of in weight_loads:
                act.dma_start(to, of).then_inc(weights_loaded, DMA)
            for s in range(LOOKUPS):
                act.wait_ge(table_loaded[s], DMA)
                nc.scalar.copy(table_hi[:, s].rearrange("p k d -> p (k d)"), raw[:, s, :]).then_inc(hi_made, 1)
            for s in range(LOOKUPS):
                copy_found(0, s)
            act.wait_ge(padded, 1)
            with act.Fori(0, chunks - 1) as c:
                for s in range(ID_SLOTS):
                    load_ids(c + 1, s)
                for t in range(TILES):
                    for g in range(TURNS):
                        copy_rows(c, t, g)
                copy_found(c + 1, 0)
                copy_pairs(c)
                copy_found(c + 1, 1)
                relu1(c)
                copy_found(c + 1, 2)
                relu2(c)
                copy_found(c + 1, 3)
                output(c)
                for s in range(4, LOOKUPS):
                    copy_found(c + 1, s)
                act.wait_ge(stored, (c + 1) * DMA)
            for t in range(TILES):
                for g in range(TURNS):
                    copy_rows(chunks - 1, t, g)
            copy_pairs(chunks - 1)
            relu1(chunks - 1)
            relu2(chunks - 1)
            output(chunks - 1)
            act.wait_ge(stored, chunks * DMA)

        @block.vector
        def _(dve):
            def one_hots(c, s, k0, k1):
                for k in range(k0, k1):
                    n = s * K_ROWS + k
                    if k == 0:
                        dve.wait_ge(ids_loaded[s], (c + 1) * DMA)
                    dve.wait_ge(one_hot_used, (c + 1) * HOTS + n - HOT_SLOTS + 1)
                    nc.vector.tensor_scalar(one_hot[:, n % HOT_SLOTS, :], table_ids[:, s % ID_SLOTS, :],
                                            row_number[:, k:k + 1], None, ALU.is_equal).then_inc(one_hot_made, 1)

            def place_found(c, t):
                dve.wait_ge(found_copied, (c + 2) * LOOKUPS)
                to = turned[:, t % 2].rearrange("p i (q f) -> p f q i", q=GROUP)[:, ROWS:FEATURES]
                of = looked_up[:, :, t * P:(t + 1) * P].rearrange("p s (q i) -> p s q i", q=GROUP)
                nc.vector.tensor_copy(to, of).then_inc(found_placed, 1)

            def copy_products(c, t):
                for u in range(UNITS):
                    n = t * UNITS + u
                    dve.wait_ge(gram_done, c * ALL_UNITS + n + 1)
                    for q in range(GROUP):
                        part = slice(q * SLOT, q * SLOT + FEATURES)
                        of = gram_bank[n % 2][part, :, 0:PER_BANK * WIDE].rearrange(
                            "p b (k q f) -> p b k q f", k=PER_BANK, q=GROUP)[:, :, :, q]
                        to = gram[part, n * UNIT:(n + 1) * UNIT, :].rearrange("p (b k) f -> p b k f", b=UNIT_BANKS)
                        last = nc.vector.tensor_copy(to, of)
                    last.then_inc(gram_copied, 1)

            def copy_cols(c):
                for g in range(COLS_TURNS):
                    dve.wait_ge(cols_turned, c * COLS_TURNS + g + 1)
                    for i in range(g * TURN, min((g + 1) * TURN, FEATURES - 1)):
                        of = late_bank[g % 2][:, i % TURN * P:(i % TURN + 1) * P].rearrange("p (q f) -> p q f", q=GROUP)
                        last = nc.vector.tensor_copy(pairs[:, :, offset(i):offset(i + 1)], of[:, :, i + 1:FEATURES])
                    last.then_inc(cols_copied, 1)

            def tiles(c):
                place_found(c, 0)
                for t in range(TILES):
                    if t + 1 < TILES:
                        place_found(c, t + 1)
                    copy_products(c, t)

            dve.sem_inc(gram_copied, ALL_UNITS)
            dve.sem_inc(cols_copied, COLS_TURNS)
            dve.sem_inc(one_hot_used, HOTS)
            dve.wait_ge(numbers_made, 1)
            nc.vector.tensor_copy(row_number[:], row_number_int[:]).then_inc(numbers_ready, 1)
            dve.wait_ge(numbers_ready, 1)
            one_hots(0, 0, 0, HOT_SLOTS)
            for s in range(LOOKUPS):
                dve.wait_ge(hi_made, s + 1)
                nc.vector.tensor_tensor(table_lo[:, s].rearrange("p k d -> p (k d)"), raw[:, s, :],
                                        table_hi[:, s].rearrange("p k d -> p (k d)").bitcast(F32), ALU.subtract).then_inc(lo_made, 1)
                one_hots(0, s, HOT_SLOTS if s == 0 else 0, K_ROWS)
            dve.wait_ge(lo_made, LOOKUPS)
            pads = turned[:].rearrange("p a i (q f) -> p (a i q) f", q=GROUP)[:, :, FEATURES:SLOT]
            nc.vector.memset(pads, 0.0).then_inc(padded, 1)
            dve.wait_ge(weights_loaded, len(weight_loads) * DMA)
            nc.vector.tensor_tensor(w1_dense[:], w1_dense[:], w1_again, ALU.add).then_inc(w1_merged, 1)
            dve.wait_ge(w1_merged, 1)
            with dve.Fori(0, chunks - 1) as c:
                tiles(c)
                one_hots(c + 1, 0, 0, HOT_SLOTS)
                copy_cols(c)
                one_hots(c + 1, 0, HOT_SLOTS, K_ROWS)
                for s in range(1, LOOKUPS):
                    one_hots(c + 1, s, 0, K_ROWS)
            tiles(chunks - 1)
            copy_cols(chunks - 1)


_TABLES = [f"tbl_{i}" for i in range(26)]
_INS = ["r_dense_features", "ids", *_TABLES, "W_top1", "b_top1", "W_top2", "b_top2", "W_top3"]
_BY_PARTITION = ("b_top1", "b_top2", "W_top3")


def _rows_by_slot(d):
    at = {}
    for a in range(FEATURES):
        for b in range(a + 1, FEATURES):
            at[a, b] = d + len(at)
    table = [0] + [1 + f for f in GATHERED + LOOKED_UP]
    order = [at[tuple(sorted((table[a], table[b])))] for a in range(FEATURES) for b in range(a + 1, FEATURES)]
    return list(range(d)) + order + list(range(d + PAIRS, d + PAIRS + d))


def kernel(**inputs):
    import numpy as _np
    import concourse.bacc as _bacc
    from concourse import mybir as _mybir
    from concourse.bass_utils import run_bass_kernel_spmd as _run

    nc = _bacc.Bacc("TRN2", target_bir_lowering=False, num_devices=1, dynamic_dma_scratch_size=8192)
    given = {name: _np.asarray(inputs[name]) for name in _INS}
    for name in _BY_PARTITION:
        given[name] = given[name].reshape(-1, P).T
    given["W_top1"] = given["W_top1"][_rows_by_slot(given["r_dense_features"].shape[1])]
    given["ids_by_table"] = given["ids"].T
    arrays, args = {}, {}
    for name, a in given.items():
        a = _np.ascontiguousarray(a)
        arrays[f"in_{name}_dram"] = a
        args[name] = nc.dram_tensor(f"in_{name}_dram", a.shape, _mybir.dt.from_np(a.dtype), kind="ExternalInput").ap()
    shape = (given["r_dense_features"].shape[0], 1)
    out = nc.dram_tensor("out_0_dram", shape, F32, kind="ExternalOutput").ap()
    dlrm_tower(nc, args["r_dense_features"], args["ids"], args["ids_by_table"], [args[n] for n in _TABLES],
               args["W_top1"], args["b_top1"], args["W_top2"], args["b_top2"], args["W_top3"], out)
    r = _run(nc, [arrays], core_ids=[0])
    return r.results[0]["out_0_dram"]
```

```python
from contextlib import ExitStack

import concourse.bass as bass
from concourse import mybir

F32 = mybir.dt.float32
F32R = mybir.dt.float32r
I32 = mybir.dt.int32
ALU = mybir.AluOpType
ACT = mybir.ActivationFunctionType

P = 128
LOOKED_UP = (6, 9, 15, 16, 17, 18, 20)
GATHERED = tuple(f for f in range(26) if f not in LOOKED_UP)
FEATURES = 1 + len(GATHERED) + len(LOOKED_UP)
ROWS = 1 + len(GATHERED)
LOOKUPS = len(LOOKED_UP)
PAIRS = FEATURES * (FEATURES - 1) // 2
LATER = FEATURES - 1
BANK = 512

TILES = 4
CHUNK = TILES * P
GROUP = 4
GROUPS = P // GROUP
TALL = GROUP * FEATURES
WIDE = GROUP * LATER
PARTS = [slice(64 if q * FEATURES >= 64 else 0, (q + 1) * FEATURES) for q in range(GROUP)]

TURN = BANK // P
TURNS = -(-ROWS // TURN)
UNIT_BANKS = 2
PER_BANK = BANK // WIDE
UNIT = UNIT_BANKS * PER_BANK
UNITS = GROUPS // UNIT
COLS_TURNS = -(-LATER // TURN)

K_PAIRS = 3
PK = PAIRS // K_PAIRS
K1 = 1 + K_PAIRS
K_ROWS = 8
HOTS = LOOKUPS * K_ROWS
H1_SLOTS = 2
HOT_SLOTS = 4
ID_SLOTS = 2
BLOCKS = {
    ("unit", 2, 0): 4, ("unit", 2, 1): 4, ("unit", 2, 2): 4, ("unit", 2, 3): 4,
    ("unit", 3, 0): 4, ("unit", 3, 1): 4, ("unit", 3, 2): 4, ("unit", 3, 3): 4,
    ("columns", 6): 4, ("pairs", 2): 4,
    ("layer1", 0): 4, ("layer1", 1): 4, ("layer1", 2): 4, ("layer1", 3): 4,
}
FIRST_HOTS = ("unit", 1, 2)
LATE = 4
assert sum(BLOCKS.values()) == HOTS and sum(n for step, n in BLOCKS.items() if step[0] == "unit") == LATE * K_ROWS
STEPS = ([("unit", t, u) for t in range(TILES) for u in range(UNITS)] + [("columns", g) for g in range(COLS_TURNS)]
         + [("pairs", k) for k in range(K_PAIRS)] + [("layer1", n) for n in range(4)])
LAYER2_AFTER = ((), (0,), (), (1, 2))
DMA = 16


def offset(row):
    return row * FEATURES - row * (row + 1) // 2


def turn_range(g):
    return g * TURN, min((g + 1) * TURN, ROWS)


def turns_before(u, awaited):
    if awaited and u >= UNITS - 1:
        return range(TURNS - 1, TURNS - 1 + (u == UNITS))
    return range(-(-u * TURNS // UNITS), min(-(-(u + 1) * TURNS // UNITS), TURNS))


def blocks_before(step):
    return sum(BLOCKS.get(before, 0) for before in STEPS[:STEPS.index(step)])


def blocks_after(*step):
    return range(blocks_before(step), blocks_before(step) + BLOCKS.get(step, 0))


def hots_after(*step):
    ahead = [min(n + HOT_SLOTS, HOTS) for n in (blocks_before(step), blocks_before(step) + BLOCKS.get(step, 0))]
    if STEPS.index(step) <= STEPS.index(FIRST_HOTS):
        return range(ahead[1] if step == FIRST_HOTS else 0)
    return range(ahead[0], ahead[1])


def dlrm_tower(nc, dense, ids, ids_t, tables, w1, b1, w2, b2, w3, out):
    B, D = dense.shape
    H1, H2 = w1.shape[1], w2.shape[1]
    N1, N2 = H1 // P, H2 // P
    chunks = B // CHUNK
    RK = tables[LOOKED_UP[0]].shape[0] // K_ROWS
    assert D == P and PK * K_PAIRS == PAIRS and B % CHUNK == 0
    assert all(tables[f].shape[0] == RK * K_ROWS for f in LOOKED_UP) and K_ROWS % HOT_SLOTS == 0
    first_pair, dense_again = D, D + PAIRS
    ALL_TURNS, ALL_UNITS = TILES * TURNS, TILES * UNITS
    COLS_STEPS = (-(-COLS_TURNS // 2), COLS_TURNS // 2)

    with ExitStack() as ctx:
        def sb(name, shape, dt=F32):
            return ctx.enter_context(nc.sbuf_tensor(name, shape, dt))

        def sem(name):
            return ctx.enter_context(nc.semaphore(name))

        ident = sb("ident", [P, P])
        w1_hi = sb("w1_hi", [P, K1, H1], F32R)
        w1_lo = sb("w1_lo", [P, K1, H1], F32R)
        w2_hi = sb("w2_hi", [P, N1, H2], F32R)
        w2_lo = sb("w2_lo", [P, N1, H2], F32R)
        w3_sb = sb("w3_sb", [P, N2])
        b1_sb = sb("b1_sb", [P, N1])
        b2_sb = sb("b2_sb", [P, N2])
        table_hi = sb("table_hi", [RK, LOOKUPS, K_ROWS, D], F32R)
        table_lo = sb("table_lo", [RK, LOOKUPS, K_ROWS, D], F32R)
        row_number = sb("row_number", [RK, K_ROWS])
        row_number_int = sb("row_number_int", [RK, K_ROWS], I32)

        index = sb("index", [P, TILES, 26], I32)
        rows = sb("rows", [P, TILES, ROWS, D])
        turned = sb("turned", [P, 2, GROUPS, TALL])
        table_ids = sb("table_ids", [RK, ID_SLOTS, CHUNK], I32)
        one_hot = sb("one_hot", [RK, HOT_SLOTS, CHUNK], F32R)
        looked_up = sb("looked_up", [P, LOOKUPS, CHUNK])
        input_hi = sb("input_hi", [P, K1, CHUNK], F32R)
        input_lo = sb("input_lo", [P, K1, CHUNK], F32R)
        gram = sb("gram", [P, TILES * GROUPS, LATER])
        h1_hi = sb("h1_hi", [P, H1_SLOTS, CHUNK], F32R)
        h1_lo = sb("h1_lo", [P, H1_SLOTS, CHUNK], F32R)
        h2 = sb("h2", [P, N2, CHUNK])
        pairs = turned[:, (TILES - 1) % 2].rearrange("p i f -> p (i f)")[:, 0:GROUP * PAIRS].rearrange("p (q f) -> p q f", q=GROUP)
        h1_whole = gram[:].rearrange("p a f -> p (a f)")[:, 0:N1 * CHUNK].rearrange("p (n b) -> p n b", n=N1)
        y = h2[0:1, 0, :]
        raw = [room[0:RK, n * K_ROWS * D:(n + 1) * K_ROWS * D]
               for room in (turned[:].rearrange("p a i f -> p (a i f)"), h2[:].rearrange("p n b -> p (n b)"))
               for n in range(room.shape[1] // (K_ROWS * D))][0:LOOKUPS]
        w1_raw = gram[:].rearrange("p a f -> p (a f)")[:, 0:(K1 + 1) * H1].rearrange("p (k n) -> p k n", k=K1 + 1)
        w2_raw = looked_up[:, LOOKUPS - 2:LOOKUPS].rearrange("p s b -> p (s b)")
        assert N1 * H2 == 2 * CHUNK

        turn_bank = [ctx.enter_context(nc.psum_tensor(f"turn_bank{i}", [P, TURN, P], F32)) for i in range(2)]
        gram_bank = [ctx.enter_context(nc.psum_tensor(f"gram_bank{i}", [P, UNIT_BANKS, BANK], F32)) for i in range(2)]
        late_bank = [ctx.enter_context(nc.psum_tensor(f"late_bank{i}", [P, BANK], F32)) for i in range(2)]

        ident_made = sem("ident_made")
        numbers_made = sem("numbers_made")
        numbers_ready = sem("numbers_ready")
        weights_loaded = sem("weights_loaded")
        table_loaded = [sem(f"table_loaded{s}") for s in range(LOOKUPS)]
        hi_made = sem("hi_made")
        lo_made = sem("lo_made")
        w1_merged = sem("w1_merged")
        w1_hi_made = sem("w1_hi_made")
        w1_lo_made = sem("w1_lo_made")
        w2_hi_made = sem("w2_hi_made")
        w2_lo_made = sem("w2_lo_made")
        index_loaded = [sem(f"index_loaded{t}") for t in range(TILES)]
        dense_loaded = [sem(f"dense_loaded{t}") for t in range(TILES)]
        ids_loaded = [sem(f"ids_loaded{s}") for s in range(LOOKUPS)]
        gathers_begun = sem("gathers_begun")
        gathered = [[sem(f"gathered{t}_{g}") for g in range(TURNS)] for t in range(TILES)]
        one_hot_made = sem("one_hot_made")
        one_hot_used = sem("one_hot_used")
        found_copied = sem("found_copied")
        found_placed = sem("found_placed")
        rows_turned = sem("rows_turned")
        rows_copied = sem("rows_copied")
        gram_done = sem("gram_done")
        part_copied = [sem(f"part_copied{i}") for i in range(2)]
        gram_copied = [sem(f"gram_copied{i}") for i in range(2)]
        cols_turned = sem("cols_turned")
        cols_copied = [sem(f"cols_copied{i}") for i in range(2)]
        pairs_turned = sem("pairs_turned")
        pairs_hi_made = sem("pairs_hi_made")
        pairs_split = sem("pairs_split")
        dense_hi_made = sem("dense_hi_made")
        dense_split = sem("dense_split")
        h1_summed = sem("h1_summed")
        h1_made = sem("h1_made")
        h1_hi_made = sem("h1_hi_made")
        h1_split = sem("h1_split")
        h1_used = sem("h1_used")
        h2_summed = sem("h2_summed")
        h2_made = sem("h2_made")
        y_summed = sem("y_summed")
        y_copied = sem("y_copied")
        stored = sem("stored")

        w1_rows = w1[first_pair:first_pair + PAIRS, :].rearrange("(k p) n -> p k n", p=PK)
        weight_loads = [
            (w1_raw[:, 0, :], w1[0:D, :]),
            (w1_raw[0:PK, 1:K1, :], w1_rows),
            (w1_raw[:, K1, :], w1[dense_again:dense_again + D, :]),
            (w2_raw.rearrange("p (k n) -> p k n", k=N1), w2.rearrange("(k p) n -> p k n", p=P)),
            (w3_sb[:], w3),
            (b1_sb[:], b1),
            (b2_sb[:], b2),
        ]
        index_tiles = ids.rearrange("(n p) f -> n p f", p=P)
        dense_tiles = dense.rearrange("(n p) d -> n p d", p=P)
        free_bank = [gram_bank[i][:, b, :] for b in range(UNIT_BANKS) for i in range(2)]
        whole_turn_bank = [turn_bank[i][:].rearrange("p f b -> p (f b)") for i in range(2)]
        cols_bank = [*whole_turn_bank, *free_bank, whole_turn_bank[0]]
        pairs_bank = free_bank[0:K_PAIRS]
        h1_bank = [late_bank[n % 2][:] for n in range(N1)]
        h2_bank = [free_bank[K_PAIRS], free_bank[0]]
        y_bank = late_bank[0][0:1, :]
        assert len(cols_bank) == COLS_TURNS and len(h2_bank) == N2 and len(LAYER2_AFTER) == N1

        def copy_products(engine, c, n):
            mine = int(engine is nc.scalar)
            copy = nc.scalar.copy if mine else nc.vector.tensor_copy
            engine.wait_ge(gram_done, c * ALL_UNITS + n + 1)
            for q in reversed(range(GROUP)):
                of = gram_bank[mine][PARTS[q], :, 0:PER_BANK * WIDE].rearrange(
                    "p b (k q f) -> p b k q f", k=PER_BANK, q=GROUP)[:, :, :, q]
                to = gram[PARTS[q], n * UNIT:(n + 1) * UNIT, :].rearrange("p (b k) f -> p b k f", b=UNIT_BANKS)
                last = copy(to, of)
                if q > 0:
                    last.then_inc(part_copied[mine], 1)
                    engine.wait_ge(part_copied[mine], (c * ALL_UNITS // 2 + n // 2) * (GROUP - 1) + GROUP - q)
            last.then_inc(gram_copied[mine], 1)

        def copy_cols(engine, c, g):
            copy = nc.scalar.copy if g % 2 else nc.vector.tensor_copy
            if g < 2:
                engine.wait_ge(dense_split, (c + 2) * TILES)
            engine.wait_ge(cols_turned, c * COLS_TURNS + g + 1)
            for i in range(g * TURN, min((g + 1) * TURN, LATER)):
                of = cols_bank[g][:, i % TURN * P:i % TURN * P + TALL].rearrange("p (q f) -> p q f", q=GROUP)
                last = copy(pairs[:, :, offset(i):offset(i + 1)], of[:, :, i + 1:FEATURES])
            last.then_inc(cols_copied[g % 2], 1)

        def found_bank(s):
            return late_bank[s % 2][:] if s < LATE else whole_turn_bank[(s + 1) % 2]

        def height(k):
            return P if k == 0 else PK

        block = ctx.enter_context(nc.Block())

        @block.sync
        def _(sp):
            def load_tile(c, t):
                sp.wait_ge(rows_copied, c * ALL_TURNS + (t + 1) * TURNS)
                of = bass.ds(c * TILES + t, 1)
                sp.dma_start(index[:, t, :], index_tiles[of].rearrange("n p f -> p (n f)")).then_inc(index_loaded[t], DMA)
                sp.dma_start(rows[:, t, 0, :], dense_tiles[of].rearrange("n p d -> p (n d)")).then_inc(dense_loaded[t], DMA)

            def load_ids(c, s):
                if s >= ID_SLOTS:
                    sp.wait_ge(one_hot_made, c * HOTS + (s - ID_SLOTS + 1) * K_ROWS)
                sp.dma_start(table_ids[:, s % ID_SLOTS, :],
                             ids_t[LOOKED_UP[s], bass.ds(c * CHUNK, CHUNK)].partition_broadcast(RK)).then_inc(ids_loaded[s], DMA)

            def store(c):
                sp.wait_ge(y_copied, c + 2)
                sp.dma_start(out[bass.ds(c * CHUNK, CHUNK), :].rearrange("b n -> n b"), y).then_inc(stored, DMA)

            load_tile(0, 0)
            for s in range(LOOKUPS):
                sp.dma_start(raw[s], tables[LOOKED_UP[s]].rearrange("(p k) d -> p (k d)", k=K_ROWS)).then_inc(table_loaded[s], DMA)
                if s < ID_SLOTS:
                    load_ids(0, s)
                if s == 2:
                    load_tile(0, 1)
            load_ids(0, ID_SLOTS)
            for to, of in weight_loads:
                sp.dma_start(to, of).then_inc(weights_loaded, DMA)
            for s in range(ID_SLOTS + 1, LOOKUPS):
                load_ids(0, s)
            for t in range(2, TILES):
                load_tile(0, t)
            with sp.Fori(1, chunks) as c:
                load_tile(c, 0)
                sp.wait_ge(one_hot_made, c * HOTS)
                for s in range(ID_SLOTS):
                    load_ids(c, s)
                load_tile(c, 1)
                load_tile(c, 2)
                load_ids(c, ID_SLOTS)
                load_tile(c, 3)
                for s in range(ID_SLOTS + 1, LOOKUPS):
                    load_ids(c, s)
                store(c - 1)
            store(chunks - 1)
            sp.wait_ge(stored, (chunks + 1) * DMA)

        @block.gpsimd
        def _(pool):
            pool.memset(ident[:], 0.0).then_inc(ident_made, 1)
            pool.iota(row_number_int[:], pattern=[[1, K_ROWS]], base=0, channel_multiplier=K_ROWS).then_inc(numbers_made, 1)
            pool.wait_ge(ident_made, 1)
            pool.affine_select(out=ident[:], in_=ident[:], compare_op=ALU.not_equal, fill=1.0, base=0,
                               pattern=[[-1, P]], channel_multiplier=1).then_inc(ident_made, 1)
            with pool.Fori(0, chunks) as c:
                for t in range(TILES):
                    pool.wait_ge(index_loaded[t], (c + 1) * DMA)
                    pool.sem_inc(gathers_begun, 1)
                    for n, f in enumerate(GATHERED):
                        pool.indirect_dma_start(
                            out=rows[:, t, n + 1, :], out_offset=None, in_=tables[f],
                            in_offset=bass.IndirectOffsetOnAxis(ap=index[:, t, f:f + 1], axis=0),
                        ).then_inc(gathered[t][(n + 1) // TURN], DMA)

        @block.tensor
        def _(pe):
            def look_up(c, blocks):
                for n in blocks:
                    s, k = divmod(n, K_ROWS)
                    if k == 0 and s >= LATE:
                        pe.wait_ge(rows_copied, (c + 1) * ALL_TURNS)
                    if k == 0 and s >= 2:
                        pe.wait_ge(found_copied, (c + 1) * LOOKUPS + s - 1)
                    pe.wait_ge(one_hot_made, c * HOTS + n + 1)
                    hot = one_hot[:, n % HOT_SLOTS, :]
                    bank = found_bank(s)
                    pe.matmul(bank, table_hi[:, s, k, :], hot, start=k == 0, stop=False)
                    pe.matmul(bank, table_lo[:, s, k, :], hot, start=False, stop=k == K_ROWS - 1).then_inc(one_hot_used, 1)

            def turn_rows(c, t, turns):
                for g in turns:
                    n = t * TURNS + g
                    f0, f1 = turn_range(g)
                    if g == 0:
                        pe.wait_ge(dense_loaded[t], (c + 1) * DMA)
                        pe.wait_ge(found_copied, (c + 2) * LOOKUPS)
                    pe.wait_ge(gathered[t][g], (c + 1) * DMA * (f1 - f0 - (g == 0)))
                    pe.wait_ge(rows_copied, (c + 1) * ALL_TURNS + n - 1)
                    for f in range(f0, f1):
                        last = pe.transpose(turn_bank[n % 2][:, f - f0, :], rows[:, t, f, :], ident[:])
                    last.then_inc(rows_turned, 1)

            def products(c, t, u):
                if u == 0:
                    pe.wait_ge(rows_copied, (c + 1) * ALL_TURNS + (t + 1) * TURNS)
                    pe.wait_ge(found_placed, (c + 1) * TILES + t + 1)
                n = t * UNITS + u
                pe.wait_ge(gram_copied[n % 2], (c + 1) * (ALL_UNITS // 2) + n // 2)
                for k in range(UNIT):
                    bank, col = k // PER_BANK, k % PER_BANK * WIDE
                    group = turned[:, t % 2, u * UNIT + k]
                    last = pe.matmul(gram_bank[n % 2][0:TALL, bank, col:col + WIDE], group,
                                     group.rearrange("p (q f) -> p q f", q=GROUP)[:, :, 0:LATER],
                                     start=True, stop=True)
                last.then_inc(gram_done, 1)

            def turn_products(c, g):
                if g == 0:
                    for i in range(2):
                        pe.wait_ge(gram_copied[i], (c + 2) * (ALL_UNITS // 2))
                if g == COLS_TURNS - 1:
                    pe.wait_ge(cols_copied[0], c * COLS_STEPS[0] + 1)
                for i in range(g * TURN, min((g + 1) * TURN, LATER)):
                    last = pe.transpose(cols_bank[g][:, i % TURN * P:i % TURN * P + TALL], gram[0:TALL, :, i],
                                        ident[0:TALL, 0:TALL])
                last.then_inc(cols_turned, 1)

            def turn_pairs(c, k):
                if k == 0:
                    for i in range(2):
                        pe.wait_ge(cols_copied[i], (c + 1) * COLS_STEPS[i])
                to = pairs_bank[k][0:PK, :].rearrange("p (t q i) -> p q t i", q=GROUP, i=GROUPS)
                for q in range(GROUP):
                    last = pe.transpose(to[:, q], pairs[:, q, k * PK:(k + 1) * PK], ident[:])
                last.then_inc(pairs_turned, 1)

            def add_layer1(c, n, k):
                p, cols = height(k), slice(n * P, (n + 1) * P)
                for w, x in ((w1_hi, input_hi), (w1_hi, input_lo), (w1_lo, input_hi)):
                    last = pe.matmul(h1_bank[n], w[0:p, k, cols], x[0:p, k, :],
                                     start=k == 0 and x is input_hi and w is w1_hi, stop=k == K1 - 1 and w is w1_lo)
                return last

            def dense_ahead(c, n, more):
                if n == 0:
                    pe.wait_ge(dense_split, (c + 2) * TILES)
                    pe.wait_ge(y_copied, c + 1)
                if more:
                    pe.wait_ge(found_copied, (c + 2) * LOOKUPS + LATE - 1 + n)
                add_layer1(c, n, 0)

            def layer1(c, n):
                if n >= 2:
                    pe.wait_ge(h1_made, (c + 1) * N1 + n - 1)
                for k in range(int(n < 2), K1):
                    if n == 0:
                        pe.wait_ge(pairs_split, c * K_PAIRS + k)
                    last = add_layer1(c, n, k)
                last.then_inc(h1_summed, 1)

            def layer2(c, k):
                pe.wait_ge(h1_split, c * N1 + k + 1)
                for n in range(N2):
                    for w, x in ((w2_hi, h1_hi), (w2_hi, h1_lo), (w2_lo, h1_hi)):
                        last = pe.matmul(h2_bank[n], w[:, k, n * P:(n + 1) * P], x[:, k % H1_SLOTS, :],
                                         start=k == 0 and x is h1_hi and w is w2_hi, stop=k == N1 - 1 and w is w2_lo)
                    if k == N1 - 1:
                        last.then_inc(h2_summed, 1)
                    elif n == N2 - 1:
                        last.then_inc(h1_used, 1)

            def layer3(c):
                for k in range(N2):
                    pe.wait_ge(h2_made, (c + 1) * N2 + k + 1)
                    last = pe.matmul(y_bank, w3_sb[:, k:k + 1], h2[:, k, :], start=k == 0, stop=k == N2 - 1)
                last.then_inc(y_summed, 1)

            def work_off(c, more):
                for t in range(TILES):
                    awaited = not more and t == TILES - 2
                    for u in range(UNITS):
                        if t + 1 < TILES:
                            turn_rows(c, t + 1, turns_before(u, awaited))
                        products(c, t, u)
                        if more:
                            if blocks_before(("unit", t, u)) == 0:
                                pe.wait_ge(y_copied, c + 1)
                            look_up(c + 1, blocks_after("unit", t, u))
                    if awaited:
                        turn_rows(c, t + 1, turns_before(UNITS, awaited))
                dense_ahead(c, 0, more)
                for g in range(COLS_TURNS):
                    turn_products(c, g)
                    if more:
                        if g == COLS_TURNS - 1:
                            pe.wait_ge(cols_copied[1], c * COLS_STEPS[1] + 1)
                        look_up(c + 1, blocks_after("columns", g))
                for k in range(K_PAIRS):
                    turn_pairs(c, k)
                    if more:
                        look_up(c + 1, blocks_after("pairs", k))
                dense_ahead(c, 1, more)
                for n in range(N1):
                    layer1(c, n)
                    if more:
                        look_up(c + 1, blocks_after("layer1", n))
                    for k in LAYER2_AFTER[n]:
                        layer2(c, k)
                if more:
                    turn_rows(c + 1, 0, range(0, 2))
                layer2(c, N1 - 1)
                if more:
                    turn_rows(c + 1, 0, range(2, TURNS))
                layer3(c)

            for s in range(LOOKUPS):
                pe.wait_ge(lo_made, s + 1)
                look_up(0, range(s * K_ROWS, (s + 1) * K_ROWS))
            pe.wait_ge(ident_made, 2)
            turn_rows(0, 0, range(TURNS))
            pe.wait_ge(weights_loaded, len(weight_loads) * DMA)
            pe.wait_ge(w1_lo_made, K1)
            pe.wait_ge(w2_lo_made, 1)
            with pe.Fori(0, chunks - 1) as c:
                work_off(c, True)
            work_off(chunks - 1, False)

        @block.scalar
        def _(act):
            def copy_found(c, blocks):
                for n in blocks:
                    s = n // K_ROWS
                    if n == 0:
                        act.wait_ge(found_placed, (c + 1) * TILES)
                    if n % K_ROWS == K_ROWS - 1:
                        act.wait_ge(one_hot_used, (c + 1) * HOTS + n + 1)
                        bank = found_bank(s)
                        nc.scalar.copy(looked_up[:, s, :], bank).then_inc(found_copied, 1)

            def copy_rows(c, t, turns):
                for g in turns:
                    n = t * TURNS + g
                    if g == 0:
                        act.wait_ge(dense_split, (c + 1) * TILES + t - 1)
                    act.wait_ge(rows_turned, c * ALL_TURNS + n + 1)
                    f0, f1 = turn_range(g)
                    to = turned[:, t % 2].rearrange("p i (q f) -> p f q i", q=GROUP)
                    of = turn_bank[n % 2][:, 0:f1 - f0, :].rearrange("p f (q i) -> p f q i", q=GROUP)
                    nc.scalar.copy(to[:, f0:f1], of).then_inc(rows_copied, 1)

            def copy_pairs(c, k):
                act.wait_ge(pairs_turned, c * K_PAIRS + k + 1)
                nc.scalar.copy(input_hi[0:PK, 1 + k, :], pairs_bank[k][0:PK, :]).then_inc(pairs_hi_made, 1)

            def relu1(c, n):
                act.wait_ge(h1_summed, c * N1 + n + 1)
                nc.scalar.activation(h1_whole[:, n, :], h1_bank[n], ACT.Relu,
                                     bias=b1_sb[:, n:n + 1]).then_inc(h1_made, 1)

            def relu2(c, n):
                if n == 0:
                    act.wait_ge(stored, (c + 1) * DMA)
                act.wait_ge(h2_summed, c * N2 + n + 1)
                nc.scalar.activation(h2[:, n, :], h2_bank[n], ACT.Relu,
                                     bias=b2_sb[:, n:n + 1]).then_inc(h2_made, 1)

            def copy_output(c):
                act.wait_ge(y_summed, c + 1)
                nc.scalar.copy(y, y_bank).then_inc(y_copied, 1)

            def work_off(c, more):
                for t in range(TILES):
                    awaited = not more and t == TILES - 2
                    for u in range(UNITS):
                        if t + 1 < TILES:
                            copy_rows(c, t + 1, turns_before(u, awaited))
                        if u % 2:
                            copy_products(act, c, t * UNITS + u)
                        if more:
                            copy_found(c + 1, blocks_after("unit", t, u))
                    if awaited:
                        copy_rows(c, t + 1, turns_before(UNITS, awaited))
                for g in range(COLS_TURNS):
                    if g % 2:
                        copy_cols(act, c, g)
                    if more:
                        copy_found(c + 1, blocks_after("columns", g))
                for k in range(K_PAIRS):
                    copy_pairs(c, k)
                    if more:
                        copy_found(c + 1, blocks_after("pairs", k))
                for n in range(N1):
                    relu1(c, n)
                    if more:
                        copy_found(c + 1, blocks_after("layer1", n))
                if more:
                    copy_rows(c + 1, 0, range(0, 2))
                for n in range(N2):
                    relu2(c, n)
                if more:
                    copy_rows(c + 1, 0, range(2, TURNS))
                copy_output(c)

            act.sem_inc(rows_copied, ALL_TURNS)
            act.sem_inc(found_copied, LOOKUPS)
            act.sem_inc(found_placed, TILES)
            act.sem_inc(gram_copied[1], ALL_UNITS // 2)
            act.sem_inc(h1_made, N1)
            act.sem_inc(h2_made, N2)
            act.sem_inc(y_copied, 1)
            act.sem_inc(stored, DMA)
            for s in range(LOOKUPS):
                act.wait_ge(table_loaded[s], DMA)
                nc.scalar.copy(table_hi[:, s].rearrange("p k d -> p (k d)"), raw[s]).then_inc(hi_made, 1)
            for s in range(LOOKUPS):
                if s == LOOKUPS - 2:
                    act.wait_ge(w2_lo_made, 1)
                copy_found(0, range(s * K_ROWS, (s + 1) * K_ROWS))
                if s == LOOKUPS - 3:
                    act.wait_ge(w1_merged, 1)
                    nc.scalar.copy(w2_hi[:].rearrange("p k n -> p (k n)"), w2_raw).then_inc(w2_hi_made, 1)
                    for k in range(K1):
                        nc.scalar.copy(w1_hi[0:height(k), k], w1_raw[0:height(k), k]).then_inc(w1_hi_made, 1)
            act.wait_ge(lo_made, LOOKUPS)
            act.wait_ge(w1_lo_made, K1)
            copy_rows(0, 0, range(TURNS))
            with act.Fori(0, chunks - 1) as c:
                work_off(c, True)
            work_off(chunks - 1, False)

        @block.vector
        def _(dve):
            def one_hots(c, blocks):
                for n in blocks:
                    s, k = divmod(n, K_ROWS)
                    if k == 0:
                        dve.wait_ge(ids_loaded[s], (c + 1) * DMA)
                    dve.wait_ge(one_hot_used, (c + 1) * HOTS + n - HOT_SLOTS + 1)
                    nc.vector.tensor_tensor(one_hot[:, n % HOT_SLOTS, :], table_ids[:, s % ID_SLOTS, :],
                                            row_number[:, k:k + 1].broadcast_to([RK, CHUNK]), ALU.is_equal).then_inc(one_hot_made, 1)

            def copy(to, of):
                return nc.vector.tensor_tensor(to, of, of, ALU.max)

            def place_found(c, t):
                dve.wait_ge(found_copied, (c + 2) * LOOKUPS)
                if t >= 2:
                    dve.wait_ge(gram_done, c * ALL_UNITS + (t - 1) * UNITS)
                to = turned[:, t % 2].rearrange("p i (q f) -> p f q i", q=GROUP)[:, ROWS:FEATURES]
                of = looked_up[:, :, t * P:(t + 1) * P].rearrange("p s (q i) -> p s q i", q=GROUP)
                copy(to, of).then_inc(found_placed, 1)

            def split_dense(c, t):
                samples = slice(t * P, (t + 1) * P)
                dense_t = turned[:, t % 2].rearrange("p i (q f) -> p f q i", q=GROUP)[:, 0]
                hi, lo = (part[:, 0, samples].rearrange("p (q i) -> p q i", q=GROUP) for part in (input_hi, input_lo))
                copy(hi, dense_t).then_inc(dense_hi_made, 1)
                dve.wait_ge(dense_hi_made, c * TILES + t + 1)
                nc.vector.tensor_tensor(lo, dense_t, hi.bitcast(F32), ALU.subtract).then_inc(dense_split, 1)

            def split_pairs(c, k):
                dve.wait_ge(pairs_hi_made, c * K_PAIRS + k + 1)
                nc.vector.tensor_tensor(input_lo[0:PK, 1 + k, :], pairs_bank[k][0:PK, :],
                                        input_hi[0:PK, 1 + k, :].bitcast(F32), ALU.subtract).then_inc(pairs_split, 1)

            def split_h1(c, n, more):
                if n >= H1_SLOTS:
                    dve.wait_ge(h1_used, c * (N1 - 1) + n - H1_SLOTS + 1)
                dve.wait_ge(h1_made, (c + 1) * N1 + n + 1)
                of_whole = copy if more else nc.vector.tensor_copy
                of_whole(h1_hi[:, n % H1_SLOTS, :], h1_whole[:, n, :]).then_inc(h1_hi_made, 1)
                dve.wait_ge(h1_hi_made, c * N1 + n + 1)
                nc.vector.tensor_tensor(h1_lo[:, n % H1_SLOTS, :], h1_whole[:, n, :],
                                        h1_hi[:, n % H1_SLOTS, :].bitcast(F32), ALU.subtract).then_inc(h1_split, 1)

            def work_off(c, more):
                place_found(c, 0)
                place_found(c, 1)
                for t in range(TILES):
                    for u in range(UNITS):
                        if u % 2 == 0:
                            copy_products(dve, c, t * UNITS + u)
                        if u == 0 and 0 < t < TILES - 1:
                            place_found(c, t + 1)
                        if u + 1 == UNITS:
                            split_dense(c, t)
                        if more:
                            one_hots(c + 1, hots_after("unit", t, u))
                for g in range(COLS_TURNS):
                    if g % 2 == 0:
                        copy_cols(dve, c, g)
                    if more:
                        one_hots(c + 1, hots_after("columns", g))
                for k in range(K_PAIRS):
                    split_pairs(c, k)
                    if more:
                        one_hots(c + 1, hots_after("pairs", k))
                for n in range(N1):
                    if more:
                        one_hots(c + 1, hots_after("layer1", n))
                    split_h1(c, n, more)

            dve.sem_inc(gram_copied[0], ALL_UNITS // 2)
            dve.sem_inc(one_hot_used, HOTS)
            dve.sem_inc(dense_split, TILES)
            dve.wait_ge(numbers_made, 1)
            nc.vector.tensor_copy(row_number[:], row_number_int[:]).then_inc(numbers_ready, 1)
            dve.wait_ge(numbers_ready, 1)
            one_hots(0, range(HOT_SLOTS))
            for s in range(LOOKUPS):
                dve.wait_ge(hi_made, s + 1)
                nc.vector.tensor_tensor(table_lo[:, s].rearrange("p k d -> p (k d)"), raw[s],
                                        table_hi[:, s].rearrange("p k d -> p (k d)").bitcast(F32), ALU.subtract).then_inc(lo_made, 1)
                one_hots(0, range(max(HOT_SLOTS, s * K_ROWS), (s + 1) * K_ROWS))
                if s == LOOKUPS - 3:
                    dve.wait_ge(weights_loaded, len(weight_loads) * DMA)
                    nc.vector.tensor_tensor(w1_raw[:, 0], w1_raw[:, 0], w1_raw[:, K1], ALU.add).then_inc(w1_merged, 1)
                if s == LOOKUPS - 1:
                    dve.wait_ge(w2_hi_made, 1)
                    nc.vector.tensor_tensor(w2_lo[:].rearrange("p k n -> p (k n)"), w2_raw,
                                            w2_hi[:].rearrange("p k n -> p (k n)").bitcast(F32), ALU.subtract).then_inc(w2_lo_made, 1)
                    for k in range(K1):
                        dve.wait_ge(w1_hi_made, k + 1)
                        nc.vector.tensor_tensor(w1_lo[0:height(k), k], w1_raw[0:height(k), k],
                                                w1_hi[0:height(k), k].bitcast(F32), ALU.subtract).then_inc(w1_lo_made, 1)
            dve.wait_ge(w1_lo_made, K1)
            dve.wait_ge(lo_made, LOOKUPS)
            with dve.Fori(0, chunks - 1) as c:
                work_off(c, True)
            work_off(chunks - 1, False)


_TABLES = [f"tbl_{i}" for i in range(26)]
_INS = ["r_dense_features", "ids", *_TABLES, "W_top1", "b_top1", "W_top2", "b_top2", "W_top3"]
_BY_PARTITION = ("b_top1", "b_top2", "W_top3")


def _rows_by_slot(d):
    at = {}
    for a in range(FEATURES):
        for b in range(a + 1, FEATURES):
            at[a, b] = d + len(at)
    table = [0] + [1 + f for f in GATHERED + LOOKED_UP]
    order = [at[tuple(sorted((table[a], table[b])))] for a in range(FEATURES) for b in range(a + 1, FEATURES)]
    return list(range(d)) + order + list(range(d + PAIRS, d + PAIRS + d))


def kernel(**inputs):
    import numpy as _np
    import concourse.bacc as _bacc
    from concourse import mybir as _mybir
    from concourse.bass_utils import run_bass_kernel_spmd as _run

    nc = _bacc.Bacc("TRN2", target_bir_lowering=False, num_devices=1, dynamic_dma_scratch_size=8192)
    given = {name: _np.asarray(inputs[name]) for name in _INS}
    for name in _BY_PARTITION:
        given[name] = given[name].reshape(-1, P).T
    given["W_top1"] = given["W_top1"][_rows_by_slot(given["r_dense_features"].shape[1])]
    given["ids_by_table"] = given["ids"].T
    arrays, args = {}, {}
    for name, a in given.items():
        a = _np.ascontiguousarray(a)
        arrays[f"in_{name}_dram"] = a
        args[name] = nc.dram_tensor(f"in_{name}_dram", a.shape, _mybir.dt.from_np(a.dtype), kind="ExternalInput").ap()
    shape = (given["r_dense_features"].shape[0], 1)
    out = nc.dram_tensor("out_0_dram", shape, F32, kind="ExternalOutput").ap()
    dlrm_tower(nc, args["r_dense_features"], args["ids"], args["ids_by_table"], [args[n] for n in _TABLES],
               args["W_top1"], args["b_top1"], args["W_top2"], args["b_top2"], args["W_top3"], out)
    r = _run(nc, [arrays], core_ids=[0])
    return r.results[0]["out_0_dram"]
```
